# Optimizing a Trainium2 kernel written in Bass

```python
import numpy as np
import jax
import jax.numpy as jnp

def _softmax(x, axis=-1):
    return jax.nn.softmax(x, axis=axis)

def _gelu(x):
    return jax.nn.gelu(x, approximate=True)

def _silu(x):
    return jax.nn.silu(x)

def _sigmoid(x):
    return jax.nn.sigmoid(x)

def _layernorm(x, axis=-1, eps=1e-05):
    m = jnp.mean(x, axis=axis, keepdims=True)
    v = jnp.var(x, axis=axis, keepdims=True)
    return (x - m) / jnp.sqrt(v + eps)

def _scatter_add(tgt, idx, src, axis=0):
    return tgt.at[idx].add(src)

def _segment_sum(src, seg, n):
    return jax.ops.segment_sum(src, seg, n)
kernel_name = 'mk_sandwich_d1_jaxref_r8_a57384'

def setup_inputs(seed: int=0):
    np.random.seed(seed)
    _w = jnp.asarray

    def _L0_attn_setup():
        import jax, jax.numpy as jnp
        import numpy as np
        B, S, D = (8, 256, 128)
        key = jax.random.key(seed)
        k1, k2, k3, k4 = jax.random.split(key, 4)
        x = jax.random.normal(k1, (B, S, D), dtype=jnp.float32)
        W0 = jax.random.normal(k2, (D, D), dtype=jnp.float32) / jnp.sqrt(jnp.float32(D))
        Wkv = jax.random.normal(k3, (2 * D, D), dtype=jnp.float32) / jnp.sqrt(jnp.float32(D))
        bkv = jax.random.normal(k4, (2 * D,), dtype=jnp.float32) * 0.01
        eta = jnp.float32(0.1)
        return {'x': x, 'W0': W0, 'Wkv': Wkv, 'bkv': bkv, 'eta': eta}
    _L0_attn_in = _L0_attn_setup()

    def _L0_ffn_setup():
        import jax, jax.numpy as jnp
        import numpy as np
        DIM = 128
        HIDDEN = 384
        SCALE = 1.0 / 127.0

        def _dequant(w_int, dtype):
            return w_int.astype(dtype) * jnp.asarray(SCALE, dtype)
        key = jax.random.key(seed)
        k_x, k_g, k_u, k_d = jax.random.split(key, 4)
        x = jax.random.normal(k_x, (4, 256, DIM), dtype=jnp.float32)
        w_gate = jax.random.randint(k_g, (HIDDEN, DIM), -127, 128, dtype=jnp.int32)
        w_up = jax.random.randint(k_u, (HIDDEN, DIM), -127, 128, dtype=jnp.int32)
        w_down = jax.random.randint(k_d, (DIM, HIDDEN), -127, 128, dtype=jnp.int32)
        return {'x': x, 'w_gate': w_gate, 'w_up': w_up, 'w_down': w_down}
    _L0_ffn_in = _L0_ffn_setup()
    _d = {'L0_attn_x': _L0_attn_in['x'], 'L0_attn_W0': _L0_attn_in['W0'], 'L0_attn_Wkv': _L0_attn_in['Wkv'], 'L0_attn_bkv': _L0_attn_in['bkv'], 'L0_attn_eta': _L0_attn_in['eta'], 'L0_ffn_w_gate': _L0_ffn_in['w_gate'], 'L0_ffn_w_up': _L0_ffn_in['w_up'], 'L0_ffn_w_down': _L0_ffn_in['w_down']}
    _x0 = _d['L0_attn_x']
    _d['L0_attn_x'] = jax.random.normal(jax.random.fold_in(jax.random.key(seed), 1), (16, 256, 128), dtype=_x0.dtype)
    del _x0
    return _d

def reference(L0_attn_x, L0_attn_W0, L0_attn_Wkv, L0_attn_bkv, L0_attn_eta, L0_ffn_w_gate, L0_ffn_w_up, L0_ffn_w_down):

    def _L0_attn_ref(x, W0, Wkv, bkv, eta):
        import jax, jax.numpy as jnp
        import numpy as np
        B, S, D = (8, 256, 128)
        b, s, d = x.shape
        v = jnp.einsum('bsd,ed->bse', x, Wkv[d:, :]) + bkv[d:]
        scale = 2.0 / (b * d)

        def step(W, inp):
            xt, vt = inp
            y = xt @ W.T
            err = y - vt
            gW = scale * (err.T @ xt)
            return (W - eta * gW, y)
        xs = jnp.swapaxes(x, 0, 1)
        vs = jnp.swapaxes(v, 0, 1)
        _, ys = jax.lax.scan(step, W0, (xs, vs))
        return jnp.swapaxes(ys, 0, 1)

    def _L0_ffn_ref(x, w_gate, w_up, w_down):
        import jax, jax.numpy as jnp
        import numpy as np
        DIM = 128
        HIDDEN = 384
        SCALE = 1.0 / 127.0

        def _dequant(w_int, dtype):
            return w_int.astype(dtype) * jnp.asarray(SCALE, dtype)
        wg = _dequant(w_gate, x.dtype)
        wu = _dequant(w_up, x.dtype)
        wd = _dequant(w_down, x.dtype)
        gate = jnp.einsum('bsd,hd->bsh', x, wg)
        up = jnp.einsum('bsd,hd->bsh', x, wu)
        h = jax.nn.silu(gate) * up
        return jnp.einsum('bsh,dh->bsd', h, wd)
    x = L0_attn_x
    x = x + _layernorm(_L0_attn_ref(_layernorm(x, axis=-1), L0_attn_W0, L0_attn_Wkv, L0_attn_bkv, L0_attn_eta), axis=-1)
    x = x + _layernorm(_L0_ffn_ref(_layernorm(x, axis=-1), L0_ffn_w_gate, L0_ffn_w_up, L0_ffn_w_down), axis=-1)
    return x

_drawn_inputs = setup_inputs


def setup_inputs(seed=0):
    import zlib

    import numpy as np

    out = dict(_drawn_inputs(seed))
    spreads = {}
    factors = {'L0_attn_bkv': 64.0}
    for name, (base, spread) in spreads.items():
        noise = np.random.default_rng([zlib.crc32(name.encode()), seed]).standard_normal(out[name].shape)
        drawn = base * np.exp(spread * noise) if base else spread * noise
        out[name] = jnp.asarray(drawn.astype(out[name].dtype))
    for name, factor in factors.items():
        out[name] = (out[name] * factor).astype(out[name].dtype)
    return out
```

```python
from contextlib import ExitStack

import concourse.bass as bass
from concourse import mybir

F32 = mybir.dt.float32
F32R = mybir.dt.float32r
I32 = mybir.dt.int32
ALU = mybir.AluOpType
ACT = mybir.ActivationFunctionType
AX_X = mybir.AxisListType.X


def ttt_swiglu_kernel(nc, x, w0, wkv, bkv, eta, w_gate, w_up, w_down, out):
    BATCH, SEQ, D = x.shape
    HIDDEN = w_gate.shape[0]
    P = 128
    assert D == P and P % BATCH == 0 and HIDDEN % P == 0
    TS = P // BATCH
    CHUNKS = SEQ // TS
    GC = 2
    GROUPS = CHUNKS // GC
    HT = HIDDEN // P
    RING = 3
    assert TS == 8 and HT == 3 and CHUNKS % GC == 0
    EPS = 1e-5
    QSCALE = 1.0 / 127.0
    INV_SQRT_D = float(D) ** -0.5
    NSQ_COLS = P - 2 * BATCH
    MSQ_AT = 2 * BATCH
    HALF = P // 2
    LOADS = [(0, GC), (GC, 2 * GC), (2 * GC, 4 * GC), (4 * GC, CHUNKS)]

    with ExitStack() as ctx:
        def sb(name, shape, dt=F32):
            return ctx.enter_context(nc.sbuf_tensor(name, shape, dt))

        def psum(name, shape):
            return ctx.enter_context(nc.psum_tensor(name, shape, F32))

        def sem(name):
            return ctx.enter_context(nc.semaphore(name))

        X = sb("X", [P, CHUNKS, D])
        mean_var = sb("mean_var", [P, RING, GC, 2])
        neg_mean = sb("neg_mean", [P, CHUNKS])
        neg_mean_scaled = sb("neg_mean_scaled", [P, CHUNKS])
        rstd1 = sb("rstd1", [P, CHUNKS])
        shift1 = sb("shift1", [P, CHUNKS])
        raw_stats = sb("raw_stats", [P, RING, GC, 6])
        ident = sb("ident", [P, P])
        center = sb("center", [P, P])
        mask_m = sb("mask_m", [P, GC, P])
        mask_n = sb("mask_n", [P, GC, P])
        eps_col = sb("eps_col", [P, GC])
        neg_half = sb("neg_half", [P, GC])
        table_probe = sb("table_probe", [P, GC])
        eta_col = sb("eta_col", [P, 1])
        neg_c = sb("neg_c", [P, 1])
        w0_rows = sb("w0_rows", [P, D])
        wv_rows = sb("wv_rows", [P, D])
        bias = sb("bias", [P, D])
        bias_mean = sb("bias_mean", [P, 1])
        bias_hi = sb("bias_hi", [P, D], F32R)
        bias_lo = sb("bias_lo", [P, D], F32R)
        bias_parts = sb("bias_parts", [P, D], F32R)
        half_ones = sb("half_ones", [P, P], F32R)
        half_ones_f = sb("half_ones_f", [P, P])
        UT = sb("UT", [P, D])
        WvT = sb("WvT", [P, D])
        gate_i = sb("gate_i", [P, HT, D], I32)
        up_i = sb("up_i", [P, HT, D], I32)
        down_i = sb("down_i", [P, HIDDEN], I32)
        gate_f = sb("gate_f", [P, HT, D])
        up_f = sb("up_f", [P, HT, D])
        down_f = sb("down_f", [P, HIDDEN])
        gateT = sb("gateT", [P, HT, P], F32R)
        upT = sb("upT", [P, HT, P], F32R)
        downT = sb("downT", [P, HT, D])

        xn = [sb(f"xn{k}", [P, GC, D]) for k in range(RING)]
        XT = [sb(f"XT{k}", [P, GC, P]) for k in range(RING)]
        TT = [sb(f"TT{k}", [P, GC, P]) for k in range(RING)]
        M = sb("M", [P, GC, P])
        N = sb("N", [P, GC, P])
        Nsq = sb("Nsq", [P, GC, P])
        Qs = sb("Qs", [P, GC, HALF])
        R = sb("R", [P, D])
        E = sb("E", [P, D])
        y = [sb(f"y{k}", [P, GC, D]) for k in range(RING)]
        xn3 = sb("xn3", [P, GC, D])
        x3hi = sb("x3hi", [P, GC * P], F32R)
        x3lo = sb("x3lo", [P, GC * P], F32R)
        silu = [sb(f"silu{t}", [P, GC * P]) for t in range(HT)]
        h = [sb(f"h{t}", [P, GC, P]) for t in range(HT)]
        squares = {i: sb(f"squares{i}", [P, GC, D]) for i in (2, 3, 4)}
        var1 = [sb(f"var1_{k}", [P, GC]) for k in range(RING)]
        meansq = {i: [sb(f"meansq{i}_{k}", [P, GC]) for k in range(RING)] for i in (2, 3, 4)}
        meansq_eps = {i: [sb(f"meansq_eps{i}_{k}", [P, GC]) for k in range(RING)] for i in (2, 3, 4)}
        rstd = {i: [sb(f"rstd{i}_{k}", [P, GC]) for k in range(RING)] for i in (2, 3, 4)}

        ps_tgn = psum("ps_tgn", [P, 4, P])
        ps_pq = psum("ps_pq", [P, 4, P])
        ps_chain = psum("ps_chain", [P, 4, P])
        ps_y = [psum(f"ps_y{j}", [P, 4, P]) for j in range(GC)]
        ps_ffn = [psum(f"ps_ffn{i}", [P, 4, P]) for i in range(2)]
        ps_down = psum("ps_down", [P, 4, P])

        x_loaded = [sem(f"x_loaded{i}") for i in range(len(LOADS))]
        attn_params_loaded = sem("attn_params_loaded")
        ffn_params_loaded = sem("ffn_params_loaded")
        stored = sem("stored")
        consts = sem("consts")
        scaled = sem("scaled")
        setup_psum = sem("setup_psum")
        u_updated = sem("u_updated")
        wv_ready = sem("wv_ready")
        ffn_psum = sem("ffn_psum")
        ffn_float = sem("ffn_float")
        ffn_ready = sem("ffn_ready")
        raw_done, mean_done = sem("raw_done"), sem("mean_done")
        neg_mean_done = sem("neg_mean_done")
        var1_done, rstd1_done, shift1_done = sem("var1_done"), sem("rstd1_done"), sem("shift1_done")
        xn_done = sem("xn_done")
        xt_psum, xt_done = sem("xt_psum"), sem("xt_done")
        gram_psum, m_done, n_done = sem("gram_psum"), sem("m_done"), sem("n_done")
        nsq_psum, nsq_done = sem("nsq_psum"), sem("nsq_done")
        im_done = sem("im_done")
        p_psum, p_added = sem("p_psum"), sem("p_added")
        q_psum, q_done = sem("q_psum"), sem("q_done")
        qq_psum, t_done = sem("qq_psum"), sem("t_done")
        r_psum, r_done = sem("r_psum"), sem("r_done")
        e_psum, e_done = sem("e_psum"), sem("e_done")
        du_psum = sem("du_psum")
        y_psum, y_done = sem("y_psum"), sem("y_done")
        sq_done = {i: sem(f"sq{i}_done") for i in (2, 3, 4)}
        sq_eps_done = {i: sem(f"sq{i}_eps_done") for i in (2, 3, 4)}
        rstd_done = {i: sem(f"rstd{i}_done") for i in (2, 3, 4)}
        x2_done, xn3_done = sem("x2_done"), sem("xn3_done")
        xn3_psum, x3hi_done, x3lo_done = sem("xn3_psum"), sem("x3hi_done"), sem("x3lo_done")
        gate_up_psum = sem("gate_up_psum")
        silu_done, h_done = sem("silu_done"), sem("h_done")
        down_psum = sem("down_psum")
        out_done = sem("out_done")

        def has(b, off):
            return not isinstance(b, int) or 0 <= b + off < GROUPS

        def at(b, value):
            return isinstance(b, int) and b == value

        def reached(eng, semaphore, value):
            if not isinstance(value, int) or value > 0:
                eng.wait_ge(semaphore, value)

        def run_steps(eng, step, ahead, behind):
            first_full, last_full = behind, GROUPS - 1 - ahead
            rounds = (last_full - first_full + 1) // RING
            for b in range(-ahead, first_full):
                step(b, b % RING)
            with eng.Fori(0, rounds) as i:
                for s in range(RING):
                    step(i * RING + (first_full + s), (first_full + s) % RING)
            for b in range(first_full + RING * rounds, GROUPS + behind):
                step(b, b % RING)

        x_rows = x.rearrange("b (n t) d -> t b n d", t=TS)
        out_rows = out.rearrange("b (n t) d -> t b n d", t=TS)

        block = ctx.enter_context(nc.Block())

        @block.sync
        def _(sp):
            def load_x(i):
                for n in range(*LOADS[i]):
                    sp.dma_start(X[:, n, :], x_rows[:, :, n, :]).then_inc(x_loaded[i], 16)

            load_x(0)
            sp.dma_start(eta_col[:], eta.partition_broadcast(P)).then_inc(attn_params_loaded, 16)
            sp.dma_start(w0_rows[:], w0).then_inc(attn_params_loaded, 16)
            sp.dma_start(wv_rows[:], wkv[D:2 * D, :]).then_inc(attn_params_loaded, 16)
            sp.dma_start(bias[:], bkv[0, D:2 * D].partition_broadcast(P)).then_inc(attn_params_loaded, 16)
            load_x(1)
            sp.dma_start(gate_i[:], w_gate.rearrange("(t p) d -> p t d", p=P)).then_inc(ffn_params_loaded, 16)
            sp.dma_start(up_i[:], w_up.rearrange("(t p) d -> p t d", p=P)).then_inc(ffn_params_loaded, 16)
            sp.dma_start(down_i[:], w_down).then_inc(ffn_params_loaded, 16)
            for i in range(2, len(LOADS)):
                load_x(i)
            with sp.Fori(0, CHUNKS) as n:
                sp.wait_ge(out_done, n + 1)
                sp.dma_start(out_rows[:, :, n, :], X[:, n, :]).then_inc(stored, 16)
            sp.wait_ge(stored, 16 * CHUNKS)

        @block.gpsimd
        def _(pool):
            g = nc.gpsimd
            g.memset(ident[:], 0.0).then_inc(consts, 1)
            g.memset(mask_m[:], 1.0).then_inc(consts, 1)
            g.memset(mask_n[:], 1.0).then_inc(consts, 1)
            g.memset(eps_col[:], EPS).then_inc(consts, 1)
            g.memset(neg_half[:], -0.5).then_inc(consts, 1)
            g.memset(Nsq[:, :, NSQ_COLS:P], 0.0).then_inc(consts, 1)
            g.memset(half_ones_f[:], 2.0 / P).then_inc(consts, 1)
            pool.wait_ge(consts, 7)
            g.affine_select(out=ident[:], in_=ident[:], compare_op=ALU.not_equal, fill=1.0, base=0,
                            pattern=[[-1, P]], channel_multiplier=1).then_inc(consts, 1)
            v = mask_m[:].rearrange("p c (j i) -> p c j i", i=BATCH)
            g.affine_select(out=v, in_=v, compare_op=ALU.is_gt, fill=0.0, base=0,
                            pattern=[[0, GC], [BATCH, TS], [0, BATCH]], channel_multiplier=-1).then_inc(consts, 1)
            v = mask_n[:].rearrange("p c (j i) -> p c j i", i=BATCH)
            g.affine_select(out=v, in_=v, compare_op=ALU.is_ge, fill=0.0, base=-BATCH,
                            pattern=[[0, GC], [-BATCH, TS], [0, BATCH]], channel_multiplier=1).then_inc(consts, 1)

            def inverse_root(i, c, k):
                pool.wait_ge(sq_done[i], c * GC + GC)
                g.tensor_tensor(meansq_eps[i][k][:], meansq[i][k][:], eps_col[:], ALU.add).then_inc(sq_eps_done[i], 1)
                pool.wait_ge(sq_eps_done[i], c + 1)
                g.tensor_tensor(rstd[i][k][:], meansq_eps[i][k][:], neg_half[:], ALU.pow).then_inc(rstd_done[i], 1)

            def step(b, k):
                k1, k2 = (k - 1) % RING, (k - 2) % RING
                if has(b, -1):
                    inverse_root(2, b - 1, k1)
                if has(b, -1):
                    inverse_root(3, b - 1, k1)
                if has(b, 3):
                    a = b + 3
                    cols = bass.ds(a * GC, GC)
                    pool.wait_ge(mean_done, a * GC + GC)
                    g.tensor_tensor(var1[k][:], mean_var[:, k, :, 1], eps_col[:], ALU.add).then_inc(var1_done, 1)
                    pool.wait_ge(var1_done, a + 1)
                    g.tensor_tensor(rstd1[:, cols], var1[k][:], neg_half[:], ALU.pow).then_inc(rstd1_done, 1)
                    pool.wait_ge(rstd1_done, a + 1)
                    pool.wait_ge(neg_mean_done, 2 * a + 2)
                    g.tensor_tensor(shift1[:, cols], neg_mean[:, cols], rstd1[:, cols], ALU.mult).then_inc(shift1_done, 1)
                if has(b, 2):
                    a = b + 2
                    ident_both = ident[:].unsqueeze(1).to_broadcast([P, GC, P])
                    pool.wait_ge(m_done, a + 1)
                    g.tensor_tensor(TT[k1][:, :, :], M[:], ident_both, ALU.add).then_inc(im_done, 1)
                if has(b, -2):
                    inverse_root(4, b - 2, k2)

            run_steps(pool, step, 3, 2)

        @block.scalar
        def _(act):
            s = nc.scalar

            def square_sum(i, c, j, k, src, shift=0.0):
                s.activation(squares[i][:, j, :], src, ACT.Square, bias=shift, scale=INV_SQRT_D,
                             accum_out=meansq[i][k][:, j:j + 1]).then_inc(sq_done[i], 1)

            def silu_tile(c, t):
                act.wait_ge(gate_up_psum, c * HT + (t + 1))
                s.activation(silu[t][:], ps_ffn[t % 2][:, 0:GC, :].rearrange("p c r -> p (c r)"), ACT.Silu,
                             scale=QSCALE).then_inc(silu_done, 1)

            def evict_e(b, j):
                act.wait_ge(e_psum, b * GC + (j + 1))
                s.activation(E[:], ps_y[j][:, 0, :], ACT.Identity).then_inc(e_done, 1)

            def evict_y(b, j, k):
                act.wait_ge(y_psum, b * GC + (j + 1))
                s.activation(y[k][:, j, :], ps_y[j][:, 0, :], ACT.Identity).then_inc(y_done, 1)

            def square_y(b, j, k):
                act.wait_ge(y_done, b * GC + (j + 1))
                square_sum(2, b, j, k, y[k][:, j, :])

            def ffn_weights():
                act.wait_ge(ffn_psum, 1)
                s.activation(gateT[:], ps_ffn[0][:, 0:HT, :], ACT.Identity).then_inc(ffn_ready, 1)
                act.wait_ge(ffn_psum, 2)
                s.activation(upT[:], ps_ffn[1][:, 0:HT, :], ACT.Identity).then_inc(ffn_ready, 1)
                act.wait_ge(ffn_psum, 3)
                s.activation(downT[:], ps_down[:, 0:HT, :], ACT.Identity).then_inc(ffn_ready, 1)

            def step(b, k):
                k1, k2 = (k - 1) % RING, (k - 2) % RING
                if has(b, 2):
                    a = b + 2
                    act.wait_ge(shift1_done, a + 1)
                    reached(act, du_psum, b * GC)
                    for j in range(GC):
                        n = a * GC + j
                        s.activation(xn[k1][:, j, :], X[:, n, :], ACT.Identity, bias=shift1[:, bass.ds(n, 1)],
                                     scale=rstd1[:, bass.ds(n, 1)]).then_inc(xn_done, 1)
                if has(b, -2):
                    silu_tile(b - 2, 0)
                if has(b, 0):
                    evict_e(b, 0)
                if has(b, -2):
                    silu_tile(b - 2, 1)
                if has(b, -1):
                    for j in range(GC):
                        n = (b - 1) * GC + j
                        act.wait_ge(x2_done, n + 1)
                        square_sum(3, b - 1, j, k1, X[:, n, :], neg_mean_scaled[:, bass.ds(n, 1)])
                if has(b, 2):
                    act.wait_ge(xt_psum, b + 3)
                    s.activation(XT[k1][:], ps_tgn[:, 0:GC, :], ACT.Identity).then_inc(xt_done, 1)
                if has(b, 0):
                    evict_y(b, 0, k)
                if has(b, -2):
                    silu_tile(b - 2, 2)
                if has(b, 1):
                    act.wait_ge(q_psum, b + 2)
                    s.activation(Qs[:], ps_pq[:, 0:GC, 0:HALF], ACT.Identity).then_inc(q_done, 1)
                if has(b, 0):
                    evict_e(b, 1)
                if has(b, 0):
                    square_y(b, 0, k)
                if has(b, -2):
                    act.wait_ge(down_psum, b - 1)
                    for j in range(GC):
                        square_sum(4, b - 2, j, k2, ps_down[:, j, :])
                if has(b, -1):
                    act.wait_ge(xn3_psum, b)
                    s.activation(x3hi[:], ps_ffn[1][:, 0:GC, :].rearrange("p c r -> p (c r)"),
                                 ACT.Identity).then_inc(x3hi_done, 1)
                if at(b, 0):
                    ffn_weights()
                if has(b, 0):
                    evict_y(b, 1, k)
                if has(b, 2):
                    act.wait_ge(nsq_psum, b + 3)
                    s.activation(Nsq[:, :, 0:NSQ_COLS], ps_tgn[:, 0:GC, 0:NSQ_COLS],
                                 ACT.Identity).then_inc(nsq_done, 1)
                if has(b, 0):
                    square_y(b, 1, k)

            act.wait_ge(consts, 7)
            s.activation(table_probe[:], eps_col[:], ACT.Silu)
            run_steps(act, step, 2, 2)

        @block.vector
        def _(dve):
            v = nc.vector

            def setup():
                dve.wait_ge(attn_params_loaded, 4 * 16)
                v.tensor_tensor(w0_rows[:], w0_rows[:], wv_rows[:], ALU.subtract).then_inc(scaled, 1)
                v.tensor_reduce(bias_mean[:], bias[:], AX_X, ALU.add).then_inc(scaled, 1)
                v.tensor_scalar(neg_c[:], eta_col[:], -2.0 / (BATCH * D), None, ALU.mult).then_inc(scaled, 1)
                dve.wait_ge(consts, 10)
                v.tensor_scalar(center[:], ident[:], 1.0 / D, None, ALU.subtract).then_inc(scaled, 1)
                dve.wait_ge(scaled, 3)
                v.tensor_scalar(mask_m[:], mask_m[:], neg_c[:, 0:1], None, ALU.mult).then_inc(scaled, 1)
                v.tensor_scalar(mask_n[:], mask_n[:], neg_c[:, 0:1], None, ALU.mult).then_inc(scaled, 1)
                v.tensor_scalar(bias_mean[:], bias_mean[:], 1.0 / D, None, ALU.mult).then_inc(scaled, 1)
                dve.wait_ge(scaled, 7)
                v.tensor_scalar(bias[:], bias[:], bias_mean[:, 0:1], None, ALU.subtract).then_inc(scaled, 1)
                v.tensor_copy(half_ones[:], half_ones_f[:]).then_inc(scaled, 1)
                dve.wait_ge(scaled, 8)
                v.tensor_copy(bias_hi[:], bias[:]).then_inc(scaled, 1)
                dve.wait_ge(scaled, 10)
                v.tensor_tensor(bias_lo[:], bias[:], bias_hi[:].bitcast(F32), ALU.subtract).then_inc(scaled, 1)
                v.tensor_copy(bias_parts[0:HALF, :], bias_hi[0:HALF, :].bitcast(F32)).then_inc(scaled, 1)
                dve.wait_ge(scaled, 11)
                v.tensor_copy(bias_parts[HALF:P, :], bias_lo[HALF:P, :].bitcast(F32)).then_inc(scaled, 1)
                dve.wait_ge(setup_psum, 1)
                v.tensor_copy(UT[:], ps_y[0][:, 0, :]).then_inc(u_updated, 1)
                dve.wait_ge(setup_psum, 2)
                v.tensor_copy(WvT[:], ps_y[1][:, 0, :]).then_inc(wv_ready, 1)

            def ffn_weights():
                dve.wait_ge(ffn_params_loaded, 3 * 16)
                v.tensor_copy(gate_f[:], gate_i[:]).then_inc(ffn_float, 1)
                v.tensor_copy(up_f[:], up_i[:]).then_inc(ffn_float, 1)
                v.tensor_copy(down_f[:], down_i[:]).then_inc(ffn_float, 1)

            def evict_r(b, j):
                dve.wait_ge(r_psum, b * GC + (j + 1))
                v.tensor_tensor(R[:], ps_chain[:, 0, :], bias[:], ALU.subtract).then_inc(r_done, 1)

            def update_u(b, j):
                dve.wait_ge(du_psum, b * GC + (j + 1))
                v.scalar_tensor_tensor(out=UT[:], in0=ps_chain[:, 1, :], scalar=neg_c[:, 0:1], in1=UT[:],
                                       op0=ALU.mult, op1=ALU.add).then_inc(u_updated, 1)

            def h_tile(c, t):
                dve.wait_ge(silu_done, c * HT + (t + 1))
                v.scalar_tensor_tensor(out=h[t][:], in0=ps_ffn[t % 2][:, GC:2 * GC, :], scalar=QSCALE * QSCALE,
                                       in1=silu[t][:].rearrange("p (c r) -> p c r", c=GC),
                                       op0=ALU.mult, op1=ALU.mult).then_inc(h_done, 1)

            def step(b, k):
                k1, k2 = (k - 1) % RING, (k - 2) % RING
                if has(b, 0):
                    evict_r(b, 0)
                if has(b, 3):
                    a = b + 3
                    for i, (first, _) in enumerate(LOADS):
                        if at(a * GC, first):
                            dve.wait_ge(x_loaded[i], 16 * (LOADS[i][1] - first))
                    for j in range(GC):
                        v.bn_stats(raw_stats[:, k, j, :], X[:, a * GC + j, :]).then_inc(raw_done, 1)
                if has(b, -3):
                    c = b - 3
                    dve.wait_ge(rstd_done[4], c + 1)
                    for j in range(GC):
                        n = c * GC + j
                        v.scalar_tensor_tensor(out=X[:, n, :], in0=ps_down[:, j, :], scalar=rstd[4][k][:, j:j + 1],
                                               in1=X[:, n, :], op0=ALU.mult, op1=ALU.add).then_inc(out_done, 1)
                if has(b, 1):
                    a = b + 1
                    dve.wait_ge(im_done, a + 1)
                    dve.wait_ge(p_psum, a + 1)
                    if has(b, 3):
                        dve.wait_ge(raw_done, (b + 3) * GC + GC)
                    t_cols = TT[(k + 1) % RING][:, :, MSQ_AT:P]
                    v.tensor_tensor(t_cols, ps_pq[:, 0:GC, MSQ_AT:P], t_cols, ALU.add).then_inc(p_added, 1)
                if has(b, -1):
                    c = b - 1
                    dve.wait_ge(rstd_done[2], b)
                    dve.wait_ge(y_done, b * GC)
                    for j in range(GC):
                        n = c * GC + j
                        v.scalar_tensor_tensor(out=X[:, n, :], in0=y[k1][:, j, :], scalar=rstd[2][k1][:, j:j + 1],
                                               in1=X[:, n, :], op0=ALU.mult, op1=ALU.add).then_inc(x2_done, 1)
                if has(b, -2):
                    h_tile(b - 2, 0)
                if has(b, 0):
                    update_u(b, 0)
                if has(b, 3):
                    if not has(b, 1):
                        dve.wait_ge(raw_done, (b + 3) * GC + GC)
                    for j in range(GC):
                        v.bn_aggr(mean_var[:, k, j, :], raw_stats[:, k, j, :]).then_inc(mean_done, 1)
                if has(b, -2):
                    h_tile(b - 2, 1)
                if at(b, -1):
                    ffn_weights()
                if has(b, 3):
                    a = b + 3
                    cols = bass.ds(a * GC, GC)
                    dve.wait_ge(mean_done, a * GC + GC)
                    v.tensor_scalar(neg_mean[:, cols], mean_var[:, k, :, 0], -1.0, None,
                                    ALU.mult).then_inc(neg_mean_done, 1)
                    v.tensor_scalar(neg_mean_scaled[:, cols], mean_var[:, k, :, 0], -INV_SQRT_D, None,
                                    ALU.mult).then_inc(neg_mean_done, 1)
                if has(b, -2):
                    h_tile(b - 2, 2)
                if at(b, -3):
                    setup()
                if has(b, 0):
                    evict_r(b, 1)
                if has(b, -1):
                    c = b - 1
                    dve.wait_ge(rstd_done[3], b)
                    dve.wait_ge(x2_done, b * GC)
                    for j in range(GC):
                        n = c * GC + j
                        v.tensor_scalar(xn3[:, j, :], X[:, n, :], neg_mean[:, bass.ds(n, 1)],
                                        rstd[3][k1][:, j:j + 1], ALU.add, ALU.mult).then_inc(xn3_done, 1)
                if has(b, 2):
                    dve.wait_ge(gram_psum, b + 3)
                    v.tensor_tensor(M[:], ps_tgn[:, 0:GC, :], mask_m[:], ALU.mult).then_inc(m_done, 1)
                    v.tensor_tensor(N[:], ps_tgn[:, 0:GC, :], mask_n[:], ALU.mult).then_inc(n_done, 1)
                if has(b, 1):
                    a = b + 1
                    dve.wait_ge(qq_psum, a + 1)
                    dve.wait_ge(p_added, a + 1)
                    quarter = TT[(k + 1) % RING][0:HALF, :, HALF:P]
                    v.tensor_tensor(quarter, ps_pq[0:HALF, 0:GC, HALF:P], quarter, ALU.add).then_inc(t_done, 1)
                if has(b, 0):
                    update_u(b, 1)
                if has(b, -1):
                    dve.wait_ge(xn3_psum, b)
                    dve.wait_ge(x3hi_done, b)
                    v.tensor_tensor(x3lo[:], ps_ffn[1][:, 0:GC, :].rearrange("p c r -> p (c r)"),
                                    x3hi[:].bitcast(F32), ALU.subtract).then_inc(x3lo_done, 1)

            run_steps(dve, step, 3, 3)

        @block.tensor
        def _(pe):
            mm = nc.tensor.matmul

            def setup():
                pe.wait_ge(scaled, 4)
                mm(ps_y[0][:, 0, :], w0_rows[:], center[:], start=True, stop=True).then_inc(setup_psum, 1)
                mm(ps_y[1][:, 0, :], wv_rows[:], center[:], start=True, stop=True).then_inc(setup_psum, 1)

            def ffn_weights():
                for i, (src, dst) in enumerate(((gate_f, ps_ffn[0]), (up_f, ps_ffn[1]))):
                    pe.wait_ge(ffn_float, i + 1)
                    for t in range(HT):
                        last = nc.tensor.transpose(dst[:, t, :], src[:, t, :], ident[:])
                    last.then_inc(ffn_psum, 1)
                pe.wait_ge(ffn_float, 3)
                for t in range(HT):
                    last = mm(ps_down[:, t, :], down_f[:, t * P:(t + 1) * P], center[:], start=True, stop=True)
                last.then_inc(ffn_psum, 1)

            def chain_r(b, j, k):
                n = b * GC + j
                pe.wait_ge(u_updated, n + 1)
                pe.wait_ge(xt_done, b + 1)
                mm(ps_chain[:, 0, :], XT[k][:, j, :], UT[:], start=True, stop=True).then_inc(r_psum, 1)

            def chain_e(b, j, k):
                n = b * GC + j
                pe.wait_ge(r_done, n + 1)
                pe.wait_ge(t_done, b + 1)
                if at(n, 0):
                    pe.wait_ge(wv_ready, 1)
                reached(pe, y_done, n - 1)
                mm(ps_y[j][:, 0, :], TT[k][:, j, :], R[:], start=True, stop=False,
                   skip_group_check=True).then_inc(e_psum, 1)

            def chain_u(b, j, k):
                n = b * GC + j
                pe.wait_ge(e_done, n + 1)
                mm(ps_chain[:, 1, :], xn[k][:, j, :], E[:], start=True, stop=True).then_inc(du_psum, 1)
                mm(ps_y[j][:, 0, :], XT[k][:, j, :], WvT[:], start=False, stop=False, skip_group_check=True)
                if at(n, 0):
                    pe.wait_ge(scaled, 13)
                mm(ps_y[j][:, 0, :], half_ones[:], bias_parts[:], start=False, stop=True,
                   skip_group_check=True).then_inc(y_psum, 1)

            def gate_up(c, t):
                if t == 0:
                    pe.wait_ge(x3hi_done, c + 1)
                    pe.wait_ge(x3lo_done, c + 1)
                    if at(c, 0):
                        pe.wait_ge(ffn_ready, 3)
                if t == 0:
                    reached(pe, h_done, c * HT)
                elif t == 2:
                    pe.wait_ge(h_done, c * HT + 1)
                for half, weights in ((0, gateT), (1, upT)):
                    flat = ps_ffn[t % 2][:, half * GC:(half + 1) * GC, :].rearrange("p c r -> p (c r)")
                    mm(flat, weights[:, t, :], x3hi[:], start=True, stop=False)
                    last = mm(flat, weights[:, t, :], x3lo[:], start=False, stop=True)
                last.then_inc(gate_up_psum, 1)

            def down(c, j):
                if j == 0:
                    reached(pe, out_done, c * GC)
                for t in range(HT):
                    pe.wait_ge(h_done, c * HT + (t + 1))
                    last = mm(ps_down[:, j, :], h[t][:, j, :], downT[:, t, :], start=(t == 0), stop=(t == HT - 1))
                if j == GC - 1:
                    last.then_inc(down_psum, 1)

            def step(b, k):
                k1, kn = (k - 1) % RING, (k + 1) % RING
                if has(b, 0):
                    chain_r(b, 0, k)
                if has(b, -2):
                    gate_up(b - 2, 0)
                if has(b, 1):
                    pe.wait_ge(nsq_done, b + 2)
                    pe.wait_ge(im_done, b + 2)
                    reached(pe, t_done, b + 1)
                    for j in range(GC):
                        last = mm(ps_pq[:, j, MSQ_AT:P], Nsq[:, j, :], TT[kn][:, j, MSQ_AT:P], start=True, stop=True)
                    last.then_inc(p_psum, 1)
                if has(b, 0):
                    chain_e(b, 0, k)
                if has(b, -2):
                    gate_up(b - 2, 1)
                if has(b, 2):
                    a = b + 2
                    pe.wait_ge(xn_done, a * GC + GC)
                    reached(pe, nsq_done, b + 2)
                    if at(b, -2):
                        pe.wait_ge(consts, 10)
                    for j in range(GC):
                        last = nc.tensor.transpose(ps_tgn[:, j, :], xn[k1][:, j, :], ident[:])
                    last.then_inc(xt_psum, 1)
                if has(b, 0):
                    chain_u(b, 0, k)
                if has(b, 1):
                    pe.wait_ge(p_added, b + 2)
                    for j in range(GC):
                        last = mm(ps_pq[:, j, 0:HALF], Nsq[:, j, :], TT[kn][:, j, HALF:P], start=True, stop=True)
                    last.then_inc(q_psum, 1)
                if has(b, -2):
                    gate_up(b - 2, 2)
                if has(b, 0):
                    chain_r(b, 1, k)
                if has(b, 2):
                    pe.wait_ge(xt_done, b + 3)
                    for j in range(GC):
                        last = mm(ps_tgn[:, j, :], XT[k1][:, j, :], XT[k1][:, j, :], start=True, stop=True)
                    last.then_inc(gram_psum, 1)
                if has(b, -2):
                    down(b - 2, 0)
                if has(b, 0):
                    chain_e(b, 1, k)
                if at(b, 0):
                    ffn_weights()
                if has(b, -2):
                    down(b - 2, 1)
                if has(b, 1):
                    pe.wait_ge(q_done, b + 2)
                    for j in range(GC):
                        last = mm(ps_pq[0:HALF, j, HALF:P], Nsq[:, j, 0:HALF], Qs[:, j, :], start=True, stop=True)
                    last.then_inc(qq_psum, 1)
                if has(b, -1):
                    pe.wait_ge(xn3_done, b * GC)
                    reached(pe, h_done, b * HT - HT - 1)
                    if at(b, 1):
                        pe.wait_ge(ffn_ready, 2)
                    for j in range(GC):
                        last = nc.tensor.transpose(ps_ffn[1][:, j, :], xn3[:, j, :], ident[:])
                    last.then_inc(xn3_psum, 1)
                if has(b, 0):
                    chain_u(b, 1, k)
                if has(b, 2):
                    pe.wait_ge(m_done, b + 3)
                    pe.wait_ge(n_done, b + 3)
                    for j in range(GC):
                        last = mm(ps_tgn[:, j, 0:NSQ_COLS], M[:, j, :], N[:, j, 0:NSQ_COLS], start=True, stop=True)
                    last.then_inc(nsq_psum, 1)

            setup()
            run_steps(pe, step, 2, 2)


_NAMES = ["L0_attn_x", "L0_attn_W0", "L0_attn_Wkv", "L0_attn_bkv", "L0_attn_eta",
          "L0_ffn_w_gate", "L0_ffn_w_up", "L0_ffn_w_down"]


def kernel(**inputs):
    import numpy as np
    import concourse.bacc as bacc
    from concourse.bass_utils import run_bass_kernel_spmd

    nc = bacc.Bacc("TRN2", target_bir_lowering=False, num_devices=1)
    arrays, args = {}, []
    for name in _NAMES:
        a = np.ascontiguousarray(inputs[name])
        if a.ndim < 2:
            a = a.reshape(1, -1)
        arrays[name + "_dram"] = a
        args.append(nc.dram_tensor(name + "_dram", a.shape, mybir.dt.from_np(a.dtype), kind="ExternalInput").ap())
    shape = inputs["L0_attn_x"].shape
    out = nc.dram_tensor("out_dram", shape, F32, kind="ExternalOutput").ap()
    ttt_swiglu_kernel(nc, *args, out)
    result = run_bass_kernel_spmd(nc, [arrays], core_ids=[0])
    return result.results[0]["out_dram"]
```

```python
from contextlib import ExitStack

import concourse.bass as bass
from concourse import mybir

F32 = mybir.dt.float32
F32R = mybir.dt.float32r
I32 = mybir.dt.int32
ALU = mybir.AluOpType
ACT = mybir.ActivationFunctionType
AX_X = mybir.AxisListType.X


def ttt_swiglu_kernel(nc, x, w0, wkv, bkv, eta, w_gate, w_up, w_down, out):
    BATCH, SEQ, D = x.shape
    HIDDEN = w_gate.shape[0]
    P = 128
    assert D == P and P % BATCH == 0 and HIDDEN % P == 0
    TS = P // BATCH
    CHUNKS = SEQ // TS
    GC = 2
    GROUPS = CHUNKS // GC
    HT = HIDDEN // P
    RING = 3
    assert TS == 8 and HT == 3 and CHUNKS % GC == 0
    EPS = 1e-5
    QSCALE = 1.0 / 127.0
    INV_SQRT_D = float(D) ** -0.5
    NSQ_COLS = P - 2 * BATCH
    MSQ_AT = 2 * BATCH
    HALF = P // 2
    LOADS = [(0, GC), (GC, 2 * GC), (2 * GC, 4 * GC), (4 * GC, 6 * GC), (6 * GC, CHUNKS)]

    with ExitStack() as ctx:
        def sb(name, shape, dt=F32):
            return ctx.enter_context(nc.sbuf_tensor(name, shape, dt))

        def psum(name, shape):
            return ctx.enter_context(nc.psum_tensor(name, shape, F32))

        def sem(name):
            return ctx.enter_context(nc.semaphore(name))

        X = sb("X", [P, CHUNKS, D])
        mean_var = sb("mean_var", [P, RING, GC, 2])
        neg_mean = sb("neg_mean", [P, CHUNKS])
        neg_mean_scaled = sb("neg_mean_scaled", [P, CHUNKS])
        rstd1 = sb("rstd1", [P, CHUNKS])
        shift1 = sb("shift1", [P, CHUNKS])
        raw_stats = sb("raw_stats", [P, RING, GC, 6])
        ident = sb("ident", [P, P])
        center = sb("center", [P, P])
        mask_m = sb("mask_m", [P, GC, P])
        mask_n = sb("mask_n", [P, GC, P])
        eps_col = sb("eps_col", [P, GC])
        neg_half = sb("neg_half", [P, GC])
        table_probe = sb("table_probe", [P, GC])
        eta_col = sb("eta_col", [P, 1])
        neg_c = sb("neg_c", [P, 1])
        w0_rows = sb("w0_rows", [P, D])
        wv_rows = sb("wv_rows", [P, D])
        bias = sb("bias", [P, D])
        bias_mean = sb("bias_mean", [P, 1])
        bias_hi = sb("bias_hi", [P, D], F32R)
        bias_lo = sb("bias_lo", [P, D], F32R)
        bias_parts = sb("bias_parts", [P, D], F32R)
        half_ones = sb("half_ones", [P, P], F32R)
        half_ones_f = sb("half_ones_f", [P, P])
        UT = sb("UT", [P, D])
        WvT = sb("WvT", [P, D])
        gate_i = sb("gate_i", [P, HT, D], I32)
        up_i = sb("up_i", [P, HT, D], I32)
        down_i = sb("down_i", [P, HIDDEN], I32)
        gate_f = sb("gate_f", [P, HT, D])
        up_f = sb("up_f", [P, HT, D])
        down_f = sb("down_f", [P, HIDDEN])
        gateT = sb("gateT", [P, HT, P], F32R)
        upT = sb("upT", [P, HT, P], F32R)
        downT = sb("downT", [P, HT, D])

        xn = [sb(f"xn{k}", [P, GC, D]) for k in range(RING)]
        XT = [sb(f"XT{k}", [P, GC, P]) for k in range(RING)]
        TT = [sb(f"TT{k}", [P, GC, P]) for k in range(RING)]
        M = sb("M", [P, GC, P])
        N = sb("N", [P, GC, P])
        Nsq = sb("Nsq", [P, GC, P])
        Qs = sb("Qs", [P, GC, HALF])
        R = sb("R", [P, D])
        E = sb("E", [P, D])
        y = [sb(f"y{k}", [P, GC, D]) for k in range(RING)]
        xn3 = sb("xn3", [P, GC, D])
        x3hi = [sb(f"x3hi{i}", [P, GC, P], F32R) for i in range(2)]
        x3lo = [sb(f"x3lo{i}", [P, GC, P], F32R) for i in range(2)]
        silu = [[sb(f"silu{i}_{t}", [P, GC, P]) for t in range(HT)] for i in range(2)]
        h = [[sb(f"h{i}_{t}", [P, GC, P]) for t in range(HT)] for i in range(2)]
        squares = {i: [sb(f"squares{i}_{k}", [P, GC, D]) for k in range(2)] for i in (2, 3, 4)}
        var1 = [sb(f"var1_{k}", [P, GC]) for k in range(RING)]
        meansq = {i: [sb(f"meansq{i}_{k}", [P, GC]) for k in range(RING)] for i in (2, 3, 4)}
        meansq_eps = {i: [sb(f"meansq_eps{i}_{k}", [P, GC]) for k in range(RING)] for i in (2, 3, 4)}
        rstd = {i: [sb(f"rstd{i}_{k}", [P, GC]) for k in range(RING)] for i in (2, 3, 4)}

        ps_tgn = psum("ps_tgn", [P, 4, P])
        ps_pq = psum("ps_pq", [P, 4, P])
        ps_chain = psum("ps_chain", [P, 4, P])
        ps_y = [psum(f"ps_y{j}", [P, 4, P]) for j in range(GC)]
        ps_ffn = [psum(f"ps_ffn{i}", [P, 4, P]) for i in range(2)]
        ps_down = psum("ps_down", [P, 4, P])

        def tile_bank(c, t, j):
            if j is None:
                return ps_ffn[t % 2]
            return ((ps_ffn[0], ps_ffn[1], ps_tgn), (ps_chain, ps_pq, ps_ffn[0]))[j][t]

        def xn3t_bank(j):
            return ps_ffn[1] if j is None else (ps_pq, ps_y[1])[j]

        def down_rows(c, j):
            return (ps_y[0], ps_ffn[1])[j][:, 0, :] if is_last(c) else ps_down[:, j, :]

        x_loaded = [sem(f"x_loaded{i}") for i in range(len(LOADS))]
        attn_params_loaded = sem("attn_params_loaded")
        ffn_params_loaded = sem("ffn_params_loaded")
        stored = sem("stored")
        consts = sem("consts")
        scaled = sem("scaled")
        bias_split = sem("bias_split")
        setup_psum = sem("setup_psum")
        u_updated = sem("u_updated")
        wv_ready = sem("wv_ready")
        ffn_psum = sem("ffn_psum")
        ffn_float = sem("ffn_float")
        ffn_ready = sem("ffn_ready")
        raw_done, mean_done = sem("raw_done"), sem("mean_done")
        neg_mean_done = sem("neg_mean_done")
        var1_done, rstd1_done, shift1_done = sem("var1_done"), sem("rstd1_done"), sem("shift1_done")
        xn_done = sem("xn_done")
        xt_psum, xt_done = sem("xt_psum"), sem("xt_done")
        gram_psum, m_done, n_done = sem("gram_psum"), sem("m_done"), sem("n_done")
        nsq_psum, nsq_done = sem("nsq_psum"), sem("nsq_done")
        im_done = sem("im_done")
        p_psum, p_added = sem("p_psum"), sem("p_added")
        q_psum, q_done = sem("q_psum"), sem("q_done")
        qq_psum, t_done = sem("qq_psum"), sem("t_done")
        r_psum, r_done = sem("r_psum"), sem("r_done")
        e_psum, e_done = sem("e_psum"), sem("e_done")
        du_psum = sem("du_psum")
        y_psum, y_done = sem("y_psum"), sem("y_done")
        sq_done = {i: sem(f"sq{i}_done") for i in (2, 3, 4)}
        sq_eps_done = {i: sem(f"sq{i}_eps_done") for i in (2, 3, 4)}
        rstd_done = {i: sem(f"rstd{i}_done") for i in (2, 3, 4)}
        x2_done, xn3_done = sem("x2_done"), sem("xn3_done")
        xn3_psum, x3hi_done, x3lo_done = sem("xn3_psum"), sem("x3hi_done"), sem("x3lo_done")
        gate_up_psum = sem("gate_up_psum")
        silu_done, h_done = sem("silu_done"), sem("h_done")
        down_psum = sem("down_psum")
        out_done = sem("out_done")

        def at(c, value):
            return isinstance(c, int) and c == value

        def reached(eng, semaphore, value):
            if not isinstance(value, int) or value > 0:
                eng.wait_ge(semaphore, value)

        def chunks(j):
            return slice(0, GC) if j is None else slice(j, j + 1)

        def nth(c, j):
            return c + 1 if j is None else c + 1 + j

        def nth_tile(c, t, j):
            return c * HT + (t + 1) if j is None else (c + j) * HT + (t + 1)

        def is_last(c):
            return at(c, GROUPS - 1)

        def run_steps(eng, step, first, last):
            rounds = (last - first + 1) // RING
            with eng.Fori(0, rounds) as i:
                for s in range(RING):
                    step(i * RING + (first + s), (first + s) % RING)
            for b in range(first + RING * rounds, last + 1):
                step(b, b % RING)

        def do(part, c, *which):
            part(c, c % RING, *which)

        x_rows = x.rearrange("b (n t) d -> t b n d", t=TS)
        out_rows = out.rearrange("b (n t) d -> t b n d", t=TS)

        block = ctx.enter_context(nc.Block())

        @block.sync
        def _(sp):
            def load_x(i):
                for n in range(*LOADS[i]):
                    sp.dma_start(X[:, n, :], x_rows[:, :, n, :]).then_inc(x_loaded[i], 16)

            load_x(0)
            sp.dma_start(eta_col[:], eta.partition_broadcast(P)).then_inc(attn_params_loaded, 16)
            sp.dma_start(w0_rows[:], w0).then_inc(attn_params_loaded, 16)
            sp.dma_start(wv_rows[:], wkv[D:2 * D, :]).then_inc(attn_params_loaded, 16)
            sp.dma_start(bias[:], bkv[0, D:2 * D].partition_broadcast(P)).then_inc(attn_params_loaded, 16)
            load_x(1)
            sp.dma_start(gate_i[:], w_gate.rearrange("(t p) d -> p t d", p=P)).then_inc(ffn_params_loaded, 16)
            sp.dma_start(up_i[:], w_up.rearrange("(t p) d -> p t d", p=P)).then_inc(ffn_params_loaded, 16)
            sp.dma_start(down_i[:], w_down).then_inc(ffn_params_loaded, 16)
            for i in range(2, len(LOADS)):
                load_x(i)

            def store(n):
                sp.wait_ge(out_done, n + 1)
                sp.dma_start(out_rows[:, :, n, :], X[:, n, :]).then_inc(stored, 16)

            with sp.Fori(0, CHUNKS - 2 * GC) as n:
                store(n)
            for n in range(CHUNKS - 2 * GC, CHUNKS):
                store(n)
            sp.wait_ge(stored, 16 * CHUNKS)

        @block.gpsimd
        def _(pool):
            g = nc.gpsimd
            g.memset(ident[:], 0.0).then_inc(consts, 1)
            g.memset(mask_m[:], 1.0).then_inc(consts, 1)
            g.memset(mask_n[:], 1.0).then_inc(consts, 1)
            g.memset(eps_col[:], EPS).then_inc(consts, 1)
            g.memset(neg_half[:], -0.5).then_inc(consts, 1)
            g.memset(Nsq[:, :, NSQ_COLS:P], 0.0).then_inc(consts, 1)
            g.memset(half_ones_f[:], 2.0 / P).then_inc(consts, 1)
            pool.wait_ge(consts, 7)
            g.affine_select(out=ident[:], in_=ident[:], compare_op=ALU.not_equal, fill=1.0, base=0,
                            pattern=[[-1, P]], channel_multiplier=1).then_inc(consts, 1)
            v = mask_m[:].rearrange("p c (j i) -> p c j i", i=BATCH)
            g.affine_select(out=v, in_=v, compare_op=ALU.is_gt, fill=0.0, base=0,
                            pattern=[[0, GC], [BATCH, TS], [0, BATCH]], channel_multiplier=-1).then_inc(consts, 1)
            v = mask_n[:].rearrange("p c (j i) -> p c j i", i=BATCH)
            g.affine_select(out=v, in_=v, compare_op=ALU.is_ge, fill=0.0, base=-BATCH,
                            pattern=[[0, GC], [-BATCH, TS], [0, BATCH]], channel_multiplier=1).then_inc(consts, 1)

            def inverse_root(c, k, i, j=None):
                js = chunks(j)
                pool.wait_ge(sq_done[i], c * GC + js.stop)
                g.tensor_tensor(meansq_eps[i][k][:, js], meansq[i][k][:, js], eps_col[:, js],
                                ALU.add).then_inc(sq_eps_done[i], 1)
                pool.wait_ge(sq_eps_done[i], nth(c, j))
                g.tensor_tensor(rstd[i][k][:, js], meansq_eps[i][k][:, js], neg_half[:, js],
                                ALU.pow).then_inc(rstd_done[i], 1)

            def rstd_of_x(c, k):
                cols = bass.ds(c * GC, GC)
                pool.wait_ge(mean_done, c * GC + GC)
                g.tensor_tensor(var1[k][:], mean_var[:, k, :, 1], eps_col[:], ALU.add).then_inc(var1_done, 1)
                pool.wait_ge(var1_done, c + 1)
                g.tensor_tensor(rstd1[:, cols], var1[k][:], neg_half[:], ALU.pow).then_inc(rstd1_done, 1)
                pool.wait_ge(rstd1_done, c + 1)
                pool.wait_ge(neg_mean_done, 2 * c + 2)
                g.tensor_tensor(shift1[:, cols], neg_mean[:, cols], rstd1[:, cols], ALU.mult).then_inc(shift1_done, 1)

            def i_plus_nt(c, k):
                ident_both = ident[:].unsqueeze(1).to_broadcast([P, GC, P])
                pool.wait_ge(m_done, c + 1)
                g.tensor_tensor(TT[k][:, :, :], M[:], ident_both, ALU.add).then_inc(im_done, 1)

            def step(b, k):
                inverse_root(b - 1, (k + 2) % RING, 2)
                inverse_root(b - 1, (k + 2) % RING, 3)
                i_plus_nt(b + 2, (k + 2) % RING)
                rstd_of_x(b + 3, k)
                inverse_root(b - 2, (k + 1) % RING, 4)

            do(rstd_of_x, 0)
            do(rstd_of_x, 1)
            do(i_plus_nt, 0)
            do(rstd_of_x, 2)
            do(rstd_of_x, 3)
            do(i_plus_nt, 1)
            do(i_plus_nt, 2)
            do(inverse_root, 0, 2)
            do(inverse_root, 0, 3)
            do(i_plus_nt, 3)
            do(rstd_of_x, 4)
            run_steps(pool, step, 2, GROUPS - 1 - 3)
            do(inverse_root, GROUPS - 4, 2)
            do(inverse_root, GROUPS - 4, 3)
            do(i_plus_nt, GROUPS - 1)
            do(inverse_root, GROUPS - 5, 4)
            do(inverse_root, GROUPS - 3, 2)
            do(inverse_root, GROUPS - 3, 3)
            do(inverse_root, GROUPS - 4, 4)
            do(inverse_root, GROUPS - 2, 2)
            do(inverse_root, GROUPS - 2, 3)
            do(inverse_root, GROUPS - 1, 2, 0)
            do(inverse_root, GROUPS - 1, 2, 1)
            do(inverse_root, GROUPS - 1, 3, 0)
            do(inverse_root, GROUPS - 3, 4)
            do(inverse_root, GROUPS - 1, 3, 1)
            do(inverse_root, GROUPS - 2, 4)
            do(inverse_root, GROUPS - 1, 4, 0)
            do(inverse_root, GROUPS - 1, 4, 1)

        @block.scalar
        def _(act):
            s = nc.scalar

            def square_sum(i, c, j, k, src, shift=0.0):
                s.activation(squares[i][is_last(c)][:, j, :], src, ACT.Square, bias=shift, scale=INV_SQRT_D,
                             accum_out=meansq[i][k][:, j:j + 1]).then_inc(sq_done[i], 1)

            def silu_tile(c, k, t, j=None):
                act.wait_ge(gate_up_psum, nth_tile(c, t, j))
                s.activation(silu[is_last(c)][t][:, chunks(j), :], tile_bank(c, t, j)[:, chunks(j), :], ACT.Silu,
                             scale=QSCALE).then_inc(silu_done, 1)

            def evict_e(b, k, j):
                act.wait_ge(e_psum, b * GC + (j + 1))
                s.activation(E[:], ps_y[j][:, 0, :], ACT.Identity).then_inc(e_done, 1)

            def evict_y(b, k, j):
                act.wait_ge(y_psum, b * GC + (j + 1))
                s.activation(y[k][:, j, :], ps_y[j][:, 0, :], ACT.Identity).then_inc(y_done, 1)

            def square_y(b, k, j):
                act.wait_ge(y_done, b * GC + (j + 1))
                square_sum(2, b, j, k, y[k][:, j, :])

            def ffn_weights(i):
                act.wait_ge(ffn_psum, i + 1)
                src, dst = ((ps_ffn[0], gateT), (ps_ffn[1], upT), (ps_down, downT))[i]
                s.activation(dst[:], src[:, 0:HT, :], ACT.Identity).then_inc(ffn_ready, 1)

            def write_xn(c, k):
                act.wait_ge(shift1_done, c + 1)
                reached(act, du_psum, (c - 2) * GC)
                for j in range(GC):
                    n = c * GC + j
                    s.activation(xn[k][:, j, :], X[:, n, :], ACT.Identity, bias=shift1[:, bass.ds(n, 1)],
                                 scale=rstd1[:, bass.ds(n, 1)]).then_inc(xn_done, 1)

            def square_x2(c, k, j=None):
                for i in range(GC)[chunks(j)]:
                    n = c * GC + i
                    act.wait_ge(x2_done, n + 1)
                    square_sum(3, c, i, k, X[:, n, :], neg_mean_scaled[:, bass.ds(n, 1)])

            def evict_xt(c, k):
                act.wait_ge(xt_psum, c + 1)
                s.activation(XT[k][:], ps_tgn[:, 0:GC, :], ACT.Identity).then_inc(xt_done, 1)

            def evict_q(c, k):
                act.wait_ge(q_psum, c + 1)
                s.activation(Qs[:], ps_pq[:, 0:GC, 0:HALF], ACT.Identity).then_inc(q_done, 1)

            def square_ffn(c, k, j=None):
                act.wait_ge(down_psum, nth(c, j))
                for i in range(GC)[chunks(j)]:
                    square_sum(4, c, i, k, down_rows(c, i))

            def evict_x3hi(c, k, j=None):
                act.wait_ge(xn3_psum, nth(c, j))
                s.activation(x3hi[is_last(c)][:, chunks(j), :], xn3t_bank(j)[:, chunks(j), :],
                             ACT.Identity).then_inc(x3hi_done, 1)

            def evict_nsq(c, k):
                act.wait_ge(nsq_psum, c + 1)
                s.activation(Nsq[:, :, 0:NSQ_COLS], ps_tgn[:, 0:GC, 0:NSQ_COLS],
                             ACT.Identity).then_inc(nsq_done, 1)

            def step(b, k):
                write_xn(b + 2, (k + 2) % RING)
                silu_tile(b - 2, (k + 1) % RING, 0)
                evict_e(b, k, 0)
                silu_tile(b - 2, (k + 1) % RING, 1)
                evict_xt(b + 2, (k + 2) % RING)
                square_x2(b - 1, (k + 2) % RING)
                silu_tile(b - 2, (k + 1) % RING, 2)
                evict_y(b, k, 0)
                square_y(b, k, 0)
                evict_e(b, k, 1)
                evict_q(b + 1, (k + 1) % RING)
                square_ffn(b - 2, (k + 1) % RING)
                evict_x3hi(b - 1, (k + 2) % RING)
                evict_y(b, k, 1)
                square_y(b, k, 1)
                evict_nsq(b + 2, (k + 2) % RING)

            act.wait_ge(consts, 7)
            s.activation(table_probe[:], eps_col[:], ACT.Silu)
            do(write_xn, 0)
            do(evict_xt, 0)
            do(write_xn, 1)
            do(evict_nsq, 0)
            do(evict_xt, 1)
            do(evict_q, 0)
            do(write_xn, 2)
            do(evict_e, 0, 0)
            do(evict_nsq, 1)
            ffn_weights(0)
            do(evict_y, 0, 0)
            do(square_y, 0, 0)
            do(evict_e, 0, 1)
            do(evict_xt, 2)
            do(evict_y, 0, 1)
            do(evict_q, 1)
            ffn_weights(1)
            do(square_y, 0, 1)
            do(write_xn, 3)
            do(evict_nsq, 2)
            do(evict_e, 1, 0)
            ffn_weights(2)
            do(evict_xt, 3)
            do(square_x2, 0)
            do(evict_y, 1, 0)
            do(evict_e, 1, 1)
            do(evict_q, 2)
            do(evict_x3hi, 0)
            do(evict_y, 1, 1)
            do(square_y, 1, 0)
            do(square_y, 1, 1)
            do(evict_nsq, 3)
            run_steps(act, step, 2, GROUPS - 1 - 2)
            do(silu_tile, GROUPS - 4, 0)
            do(evict_e, GROUPS - 2, 0)
            do(silu_tile, GROUPS - 4, 1)
            do(square_x2, GROUPS - 3)
            do(evict_y, GROUPS - 2, 0)
            do(square_y, GROUPS - 2, 0)
            do(silu_tile, GROUPS - 4, 2)
            do(evict_q, GROUPS - 1)
            do(evict_e, GROUPS - 2, 1)
            do(square_ffn, GROUPS - 4)
            do(evict_x3hi, GROUPS - 3)
            do(evict_y, GROUPS - 2, 1)
            do(square_y, GROUPS - 2, 1)
            do(silu_tile, GROUPS - 3, 0)
            do(evict_e, GROUPS - 1, 0)
            do(silu_tile, GROUPS - 3, 1)
            do(square_x2, GROUPS - 2)
            do(evict_y, GROUPS - 1, 0)
            do(square_y, GROUPS - 1, 0)
            do(silu_tile, GROUPS - 3, 2)
            do(evict_e, GROUPS - 1, 1)
            do(evict_x3hi, GROUPS - 2)
            do(evict_y, GROUPS - 1, 1)
            do(square_y, GROUPS - 1, 1)
            do(square_x2, GROUPS - 1, 0)
            do(square_ffn, GROUPS - 3)
            do(silu_tile, GROUPS - 2, 0)
            do(silu_tile, GROUPS - 2, 1)
            do(square_x2, GROUPS - 1, 1)
            do(silu_tile, GROUPS - 2, 2)
            do(evict_x3hi, GROUPS - 1, 0)
            do(silu_tile, GROUPS - 1, 0, 0)
            do(evict_x3hi, GROUPS - 1, 1)
            do(silu_tile, GROUPS - 1, 1, 0)
            do(silu_tile, GROUPS - 1, 2, 0)
            do(square_ffn, GROUPS - 2)
            do(silu_tile, GROUPS - 1, 0, 1)
            do(silu_tile, GROUPS - 1, 1, 1)
            do(silu_tile, GROUPS - 1, 2, 1)
            do(square_ffn, GROUPS - 1, 0)
            do(square_ffn, GROUPS - 1, 1)

        @block.vector
        def _(dve):
            v = nc.vector

            def scale_parameters():
                dve.wait_ge(attn_params_loaded, 4 * 16)
                v.tensor_tensor(w0_rows[:], w0_rows[:], wv_rows[:], ALU.subtract).then_inc(scaled, 1)
                v.tensor_reduce(bias_mean[:], bias[:], AX_X, ALU.add).then_inc(scaled, 1)
                v.tensor_scalar(neg_c[:], eta_col[:], -2.0 / (BATCH * D), None, ALU.mult).then_inc(scaled, 1)
                dve.wait_ge(consts, 10)
                v.tensor_scalar(center[:], ident[:], 1.0 / D, None, ALU.subtract).then_inc(scaled, 1)

            def scale_masks():
                dve.wait_ge(scaled, 3)
                v.tensor_scalar(mask_m[:], mask_m[:], neg_c[:, 0:1], None, ALU.mult).then_inc(scaled, 1)
                v.tensor_scalar(mask_n[:], mask_n[:], neg_c[:, 0:1], None, ALU.mult).then_inc(scaled, 1)
                v.tensor_scalar(bias_mean[:], bias_mean[:], 1.0 / D, None, ALU.mult).then_inc(scaled, 1)
                dve.wait_ge(scaled, 7)
                v.tensor_scalar(bias[:], bias[:], bias_mean[:, 0:1], None, ALU.subtract).then_inc(scaled, 1)

            def split_bias():
                dve.wait_ge(consts, 7)
                v.tensor_copy(half_ones[:], half_ones_f[:]).then_inc(bias_split, 1)
                dve.wait_ge(scaled, 8)
                v.tensor_copy(bias_hi[:], bias[:]).then_inc(bias_split, 1)
                dve.wait_ge(bias_split, 2)
                v.tensor_tensor(bias_lo[:], bias[:], bias_hi[:].bitcast(F32), ALU.subtract).then_inc(bias_split, 1)
                v.tensor_copy(bias_parts[0:HALF, :], bias_hi[0:HALF, :].bitcast(F32)).then_inc(bias_split, 1)
                dve.wait_ge(bias_split, 3)
                v.tensor_copy(bias_parts[HALF:P, :], bias_lo[HALF:P, :].bitcast(F32)).then_inc(bias_split, 1)

            def copy_ut():
                dve.wait_ge(setup_psum, 1)
                v.tensor_copy(UT[:], ps_y[0][:, 0, :]).then_inc(u_updated, 1)

            def copy_wvt():
                dve.wait_ge(setup_psum, 2)
                v.tensor_copy(WvT[:], ps_y[1][:, 0, :]).then_inc(wv_ready, 1)

            def ffn_weights(i):
                dve.wait_ge(ffn_params_loaded, 3 * 16)
                src, dst = ((gate_i, gate_f), (up_i, up_f), (down_i, down_f))[i]
                v.tensor_copy(dst[:], src[:]).then_inc(ffn_float, 1)

            def evict_r(b, k, j):
                dve.wait_ge(r_psum, b * GC + (j + 1))
                if at(b, 0):
                    dve.wait_ge(scaled, 8)
                v.tensor_tensor(R[:], ps_chain[:, 0, :], bias[:], ALU.subtract).then_inc(r_done, 1)

            def update_u(b, k, j):
                dve.wait_ge(du_psum, b * GC + (j + 1))
                v.scalar_tensor_tensor(out=UT[:], in0=ps_chain[:, 1, :], scalar=neg_c[:, 0:1], in1=UT[:],
                                       op0=ALU.mult, op1=ALU.add).then_inc(u_updated, 1)

            def h_tile(c, k, t, j=None):
                dve.wait_ge(silu_done, nth_tile(c, t, j))
                up = slice(GC + chunks(j).start, GC + chunks(j).stop)
                v.scalar_tensor_tensor(out=h[is_last(c)][t][:, chunks(j), :], in0=tile_bank(c, t, j)[:, up, :],
                                       scalar=QSCALE * QSCALE, in1=silu[is_last(c)][t][:, chunks(j), :],
                                       op0=ALU.mult, op1=ALU.mult).then_inc(h_done, 1)

            def x_stats(c, k):
                for i, (first, end) in enumerate(LOADS):
                    if at(c * GC, first):
                        dve.wait_ge(x_loaded[i], 16 * (end - first))
                for j in range(GC):
                    v.bn_stats(raw_stats[:, k, j, :], X[:, c * GC + j, :]).then_inc(raw_done, 1)

            def x_mean_var(c, k):
                if isinstance(c, int):
                    dve.wait_ge(raw_done, c * GC + GC)
                for j in range(GC):
                    v.bn_aggr(mean_var[:, k, j, :], raw_stats[:, k, j, :]).then_inc(mean_done, 1)

            def negated_means(c, k):
                cols = bass.ds(c * GC, GC)
                dve.wait_ge(mean_done, c * GC + GC)
                v.tensor_scalar(neg_mean[:, cols], mean_var[:, k, :, 0], -1.0, None,
                                ALU.mult).then_inc(neg_mean_done, 1)
                v.tensor_scalar(neg_mean_scaled[:, cols], mean_var[:, k, :, 0], -INV_SQRT_D, None,
                                ALU.mult).then_inc(neg_mean_done, 1)

            def write_m(c, k):
                dve.wait_ge(gram_psum, c + 1)
                v.tensor_tensor(M[:], ps_tgn[:, 0:GC, :], mask_m[:], ALU.mult).then_inc(m_done, 1)

            def write_n(c, k):
                dve.wait_ge(gram_psum, c + 1)
                v.tensor_tensor(N[:], ps_tgn[:, 0:GC, :], mask_n[:], ALU.mult).then_inc(n_done, 1)

            def first_product(c, k):
                dve.wait_ge(im_done, c + 1)
                dve.wait_ge(p_psum, c + 1)
                if not isinstance(c, int):
                    dve.wait_ge(raw_done, (c + 2) * GC + GC)
                t_cols = TT[k][:, :, MSQ_AT:P]
                v.tensor_tensor(t_cols, ps_pq[:, 0:GC, MSQ_AT:P], t_cols, ALU.add).then_inc(p_added, 1)

            def second_product(c, k):
                dve.wait_ge(qq_psum, c + 1)
                dve.wait_ge(p_added, c + 1)
                quarter = TT[k][0:HALF, :, HALF:P]
                v.tensor_tensor(quarter, ps_pq[0:HALF, 0:GC, HALF:P], quarter, ALU.add).then_inc(t_done, 1)

            def write_x2(c, k, j=None):
                dve.wait_ge(rstd_done[2], nth(c, j))
                dve.wait_ge(y_done, c * GC + chunks(j).stop)
                for i in range(GC)[chunks(j)]:
                    n = c * GC + i
                    v.scalar_tensor_tensor(out=X[:, n, :], in0=y[k][:, i, :], scalar=rstd[2][k][:, i:i + 1],
                                           in1=X[:, n, :], op0=ALU.mult, op1=ALU.add).then_inc(x2_done, 1)

            def write_xn3(c, k, j=None):
                dve.wait_ge(rstd_done[3], nth(c, j))
                dve.wait_ge(x2_done, c * GC + chunks(j).stop)
                for i in range(GC)[chunks(j)]:
                    n = c * GC + i
                    v.tensor_scalar(xn3[:, i, :], X[:, n, :], neg_mean[:, bass.ds(n, 1)],
                                    rstd[3][k][:, i:i + 1], ALU.add, ALU.mult).then_inc(xn3_done, 1)

            def write_x3lo(c, k, j=None):
                dve.wait_ge(xn3_psum, nth(c, j))
                dve.wait_ge(x3hi_done, nth(c, j))
                v.tensor_tensor(x3lo[is_last(c)][:, chunks(j), :], xn3t_bank(j)[:, chunks(j), :],
                                x3hi[is_last(c)][:, chunks(j), :].bitcast(F32), ALU.subtract).then_inc(x3lo_done, 1)

            def write_result(c, k, j=None):
                dve.wait_ge(rstd_done[4], nth(c, j))
                for i in range(GC)[chunks(j)]:
                    n = c * GC + i
                    v.scalar_tensor_tensor(out=X[:, n, :], in0=down_rows(c, i), scalar=rstd[4][k][:, i:i + 1],
                                           in1=X[:, n, :], op0=ALU.mult, op1=ALU.add).then_inc(out_done, 1)

            def step(b, k):
                evict_r(b, k, 0)
                x_stats(b + 3, k)
                write_result(b - 3, k)
                h_tile(b - 2, (k + 1) % RING, 0)
                write_x2(b - 1, (k + 2) % RING)
                update_u(b, k, 0)
                first_product(b + 1, (k + 1) % RING)
                h_tile(b - 2, (k + 1) % RING, 1)
                evict_r(b, k, 1)
                h_tile(b - 2, (k + 1) % RING, 2)
                write_m(b + 2, (k + 2) % RING)
                x_mean_var(b + 3, k)
                write_xn3(b - 1, (k + 2) % RING)
                negated_means(b + 3, k)
                write_n(b + 2, (k + 2) % RING)
                update_u(b, k, 1)
                write_x3lo(b - 1, (k + 2) % RING)
                second_product(b + 1, (k + 1) % RING)

            do(x_stats, 0)
            do(x_mean_var, 0)
            do(negated_means, 0)
            scale_parameters()
            scale_masks()
            do(x_stats, 1)
            do(x_mean_var, 1)
            copy_ut()
            do(write_m, 0)
            copy_wvt()
            do(negated_means, 1)
            do(write_n, 0)
            split_bias()
            do(evict_r, 0, 0)
            do(x_stats, 2)
            do(x_mean_var, 2)
            do(negated_means, 2)
            do(first_product, 0)
            ffn_weights(0)
            do(x_stats, 3)
            do(x_mean_var, 3)
            do(negated_means, 3)
            do(write_n, 1)
            do(write_m, 1)
            do(second_product, 0)
            ffn_weights(1)
            do(x_stats, 4)
            ffn_weights(2)
            do(update_u, 0, 0)
            do(evict_r, 0, 1)
            do(first_product, 1)
            do(update_u, 0, 1)
            do(write_n, 2)
            do(write_m, 2)
            do(second_product, 1)
            do(evict_r, 1, 0)
            do(write_x2, 0)
            do(update_u, 1, 0)
            do(first_product, 2)
            do(write_m, 3)
            do(evict_r, 1, 1)
            do(write_xn3, 0)
            do(write_n, 3)
            do(x_mean_var, 4)
            do(negated_means, 4)
            do(update_u, 1, 1)
            do(write_x3lo, 0)
            do(second_product, 2)
            do(evict_r, 2, 0)
            do(x_stats, 5)
            do(write_x2, 1)
            do(h_tile, 0, 0)
            do(update_u, 2, 0)
            do(h_tile, 0, 1)
            do(first_product, 3)
            do(evict_r, 2, 1)
            do(x_mean_var, 5)
            do(h_tile, 0, 2)
            do(write_m, 4)
            do(write_xn3, 1)
            do(write_n, 4)
            do(negated_means, 5)
            do(update_u, 2, 1)
            do(write_x3lo, 1)
            do(second_product, 3)
            dve.wait_ge(x_loaded[-1], 16 * (LOADS[-1][1] - LOADS[-1][0]))
            run_steps(dve, step, 3, GROUPS - 1 - 3)
            do(evict_r, GROUPS - 3, 0)
            do(write_result, GROUPS - 6)
            do(write_x2, GROUPS - 4)
            do(h_tile, GROUPS - 5, 0)
            do(update_u, GROUPS - 3, 0)
            do(first_product, GROUPS - 2)
            do(h_tile, GROUPS - 5, 1)
            do(evict_r, GROUPS - 3, 1)
            do(h_tile, GROUPS - 5, 2)
            do(write_m, GROUPS - 1)
            do(write_n, GROUPS - 1)
            do(write_xn3, GROUPS - 4)
            do(update_u, GROUPS - 3, 1)
            do(write_x3lo, GROUPS - 4)
            do(second_product, GROUPS - 2)
            do(evict_r, GROUPS - 2, 0)
            do(write_result, GROUPS - 5)
            do(h_tile, GROUPS - 4, 0)
            do(write_x2, GROUPS - 3)
            do(update_u, GROUPS - 2, 0)
            do(h_tile, GROUPS - 4, 1)
            do(first_product, GROUPS - 1)
            do(evict_r, GROUPS - 2, 1)
            do(h_tile, GROUPS - 4, 2)
            do(write_xn3, GROUPS - 3)
            do(update_u, GROUPS - 2, 1)
            do(write_x3lo, GROUPS - 3)
            do(second_product, GROUPS - 1)
            do(evict_r, GROUPS - 1, 0)
            do(write_result, GROUPS - 4)
            do(write_x2, GROUPS - 2)
            do(h_tile, GROUPS - 3, 0)
            do(h_tile, GROUPS - 3, 1)
            do(update_u, GROUPS - 1, 0)
            do(evict_r, GROUPS - 1, 1)
            do(h_tile, GROUPS - 3, 2)
            do(write_xn3, GROUPS - 2)
            do(write_x3lo, GROUPS - 2)
            do(write_x2, GROUPS - 1, 0)
            do(write_x2, GROUPS - 1, 1)
            do(h_tile, GROUPS - 2, 0)
            do(write_xn3, GROUPS - 1, 0)
            do(h_tile, GROUPS - 2, 1)
            do(write_result, GROUPS - 3)
            do(write_xn3, GROUPS - 1, 1)
            do(h_tile, GROUPS - 2, 2)
            do(write_x3lo, GROUPS - 1, 0)
            do(h_tile, GROUPS - 1, 1, 0)
            do(h_tile, GROUPS - 1, 0, 0)
            do(h_tile, GROUPS - 1, 2, 0)
            do(write_x3lo, GROUPS - 1, 1)
            do(h_tile, GROUPS - 1, 0, 1)
            do(h_tile, GROUPS - 1, 1, 1)
            do(h_tile, GROUPS - 1, 2, 1)
            do(write_result, GROUPS - 2)
            do(write_result, GROUPS - 1, 0)
            do(write_result, GROUPS - 1, 1)

        @block.tensor
        def _(pe):
            mm = nc.tensor.matmul

            def keep_warm(times, bank=ps_down):
                for _ in range(times):
                    mm(bank[:, 3, :], half_ones_f[:], half_ones_f[:], start=True, stop=True)

            def setup(i):
                pe.wait_ge(scaled, 4)
                mm(ps_y[i][:, 0, :], (w0_rows, wv_rows)[i][:], center[:], start=True, stop=True).then_inc(setup_psum, 1)

            def ffn_weights(i):
                pe.wait_ge(ffn_float, i + 1)
                for t in range(HT):
                    if i < 2:
                        last = nc.tensor.transpose(ps_ffn[i][:, t, :], (gate_f, up_f)[i][:, t, :], ident[:])
                    else:
                        last = mm(ps_down[:, t, :], down_f[:, t * P:(t + 1) * P], center[:], start=True, stop=True)
                last.then_inc(ffn_psum, 1)

            def chain_r(b, k, j):
                n = b * GC + j
                pe.wait_ge(u_updated, n + 1)
                pe.wait_ge(xt_done, b + 1)
                mm(ps_chain[:, 0, :], XT[k][:, j, :], UT[:], start=True, stop=True).then_inc(r_psum, 1)

            def chain_e(b, k, j):
                n = b * GC + j
                pe.wait_ge(r_done, n + 1)
                pe.wait_ge(t_done, b + 1)
                if at(n, 0):
                    pe.wait_ge(wv_ready, 1)
                reached(pe, y_done, n - 1)
                mm(ps_y[j][:, 0, :], TT[k][:, j, :], R[:], start=True, stop=False,
                   skip_group_check=True).then_inc(e_psum, 1)

            def chain_u(b, k, j):
                n = b * GC + j
                pe.wait_ge(e_done, n + 1)
                if not at(n, CHUNKS - 1):
                    mm(ps_chain[:, 1, :], xn[k][:, j, :], E[:], start=True, stop=True).then_inc(du_psum, 1)
                mm(ps_y[j][:, 0, :], XT[k][:, j, :], WvT[:], start=False, stop=False, skip_group_check=True)
                if at(n, 0):
                    pe.wait_ge(bias_split, 5)
                mm(ps_y[j][:, 0, :], half_ones[:], bias_parts[:], start=False, stop=True,
                   skip_group_check=True).then_inc(y_psum, 1)

            def gate_up(c, k, t, j=None):
                bank, js = tile_bank(c, t, j), chunks(j)
                if t == 0:
                    pe.wait_ge(x3hi_done, nth(c, j))
                    pe.wait_ge(x3lo_done, nth(c, j))
                    if at(c, 0):
                        pe.wait_ge(ffn_ready, 3)
                    reached(pe, h_done, c * HT)
                elif t == 2 and j != 0:
                    pe.wait_ge(h_done, c * HT + 1)
                for at_chunk, weights in ((0, gateT), (GC, upT)):
                    flat = bank[:, at_chunk + js.start:at_chunk + js.stop, :].rearrange("p c r -> p (c r)")
                    mm(flat, weights[:, t, :], x3hi[is_last(c)][:, js, :].rearrange("p c r -> p (c r)"),
                       start=True, stop=False)
                    last = mm(flat, weights[:, t, :], x3lo[is_last(c)][:, js, :].rearrange("p c r -> p (c r)"),
                              start=False, stop=True)
                last.then_inc(gate_up_psum, 1)

            def down(c, k, j):
                if j == 0 and not is_last(c):
                    reached(pe, out_done, c * GC)
                for t in range(HT):
                    pe.wait_ge(h_done, nth_tile(c, t, j if is_last(c) else None))
                    last = mm(down_rows(c, j), h[is_last(c)][t][:, j, :], downT[:, t, :],
                              start=(t == 0), stop=(t == HT - 1))
                if j == GC - 1 or is_last(c):
                    last.then_inc(down_psum, 1)

            def x_transposed(c, k):
                pe.wait_ge(xn_done, c * GC + GC)
                reached(pe, nsq_done, c)
                if at(c, 0):
                    pe.wait_ge(consts, 10)
                for j in range(GC):
                    last = nc.tensor.transpose(ps_tgn[:, j, :], xn[k][:, j, :], ident[:])
                last.then_inc(xt_psum, 1)

            def gram(c, k):
                pe.wait_ge(xt_done, c + 1)
                for j in range(GC):
                    last = mm(ps_tgn[:, j, :], XT[k][:, j, :], XT[k][:, j, :], start=True, stop=True)
                last.then_inc(gram_psum, 1)

            def n_squared(c, k):
                pe.wait_ge(m_done, c + 1)
                pe.wait_ge(n_done, c + 1)
                for j in range(GC):
                    last = mm(ps_tgn[:, j, 0:NSQ_COLS], M[:, j, :], N[:, j, 0:NSQ_COLS], start=True, stop=True)
                last.then_inc(nsq_psum, 1)

            def t_first(c, k):
                pe.wait_ge(nsq_done, c + 1)
                pe.wait_ge(im_done, c + 1)
                reached(pe, t_done, c)
                for j in range(GC):
                    last = mm(ps_pq[:, j, MSQ_AT:P], Nsq[:, j, :], TT[k][:, j, MSQ_AT:P], start=True, stop=True)
                last.then_inc(p_psum, 1)

            def t_second(c, k):
                pe.wait_ge(p_added, c + 1)
                for j in range(GC):
                    last = mm(ps_pq[:, j, 0:HALF], Nsq[:, j, :], TT[k][:, j, HALF:P], start=True, stop=True)
                last.then_inc(q_psum, 1)

            def t_third(c, k):
                pe.wait_ge(q_done, c + 1)
                for j in range(GC):
                    last = mm(ps_pq[0:HALF, j, HALF:P], Nsq[:, j, 0:HALF], Qs[:, j, :], start=True, stop=True)
                last.then_inc(qq_psum, 1)

            def xn3_transposed(c, k, j=None):
                pe.wait_ge(xn3_done, c * GC + chunks(j).stop)
                if j is None:
                    reached(pe, h_done, c * HT - 1)
                elif j == 0:
                    pe.wait_ge(t_done, GROUPS)
                else:
                    pe.wait_ge(y_done, CHUNKS)
                if at(c, 0):
                    pe.wait_ge(ffn_ready, 2)
                for i in range(GC)[chunks(j)]:
                    last = nc.tensor.transpose(xn3t_bank(j)[:, i, :], xn3[:, i, :], ident[:])
                last.then_inc(xn3_psum, 1)

            def step(b, k):
                chain_r(b, k, 0)
                gate_up(b - 2, (k + 1) % RING, 0)
                gate_up(b - 2, (k + 1) % RING, 1)
                chain_e(b, k, 0)
                t_first(b + 1, (k + 1) % RING)
                x_transposed(b + 2, (k + 2) % RING)
                chain_u(b, k, 0)
                gate_up(b - 2, (k + 1) % RING, 2)
                chain_r(b, k, 1)
                gram(b + 2, (k + 2) % RING)
                t_second(b + 1, (k + 1) % RING)
                chain_e(b, k, 1)
                down(b - 2, (k + 1) % RING, 0)
                down(b - 2, (k + 1) % RING, 1)
                xn3_transposed(b - 1, (k + 2) % RING)
                chain_u(b, k, 1)
                t_third(b + 1, (k + 1) % RING)
                n_squared(b + 2, (k + 2) % RING)

            pe.wait_ge(consts, 7)
            keep_warm(11)
            setup(0)
            do(x_transposed, 0)
            setup(1)
            keep_warm(2)
            do(gram, 0)
            do(chain_r, 0, 0)
            keep_warm(6)
            do(n_squared, 0)
            keep_warm(3)
            do(t_first, 0)
            keep_warm(1)
            do(x_transposed, 1)
            keep_warm(1)
            do(t_second, 0)
            do(gram, 1)
            do(t_third, 0)
            keep_warm(3)
            keep_warm(1)
            do(chain_e, 0, 0)
            do(n_squared, 1)
            ffn_weights(0)
            do(chain_u, 0, 0)
            do(t_first, 1)
            do(chain_r, 0, 1)
            do(x_transposed, 2)
            keep_warm(1)
            do(chain_e, 0, 1)
            do(t_second, 1)
            do(chain_u, 0, 1)
            ffn_weights(1)
            do(gram, 2)
            do(chain_r, 1, 0)
            do(t_third, 1)
            ffn_weights(2)
            do(n_squared, 2)
            do(chain_e, 1, 0)
            do(x_transposed, 3)
            do(chain_u, 1, 0)
            do(t_first, 2)
            do(gram, 3)
            do(chain_r, 1, 1)
            do(t_second, 2)
            do(chain_e, 1, 1)
            do(xn3_transposed, 0)
            do(chain_u, 1, 1)
            do(t_third, 2)
            do(n_squared, 3)
            run_steps(pe, step, 2, GROUPS - 1 - 2)
            do(chain_r, GROUPS - 2, 0)
            do(gate_up, GROUPS - 4, 0)
            do(gate_up, GROUPS - 4, 1)
            do(chain_e, GROUPS - 2, 0)
            do(t_first, GROUPS - 1)
            do(chain_u, GROUPS - 2, 0)
            do(gate_up, GROUPS - 4, 2)
            do(chain_r, GROUPS - 2, 1)
            do(t_second, GROUPS - 1)
            do(chain_e, GROUPS - 2, 1)
            do(down, GROUPS - 4, 0)
            do(down, GROUPS - 4, 1)
            do(t_third, GROUPS - 1)
            do(xn3_transposed, GROUPS - 3)
            do(chain_u, GROUPS - 2, 1)
            do(chain_r, GROUPS - 1, 0)
            do(gate_up, GROUPS - 3, 0)
            do(chain_e, GROUPS - 1, 0)
            do(gate_up, GROUPS - 3, 1)
            do(chain_u, GROUPS - 1, 0)
            do(gate_up, GROUPS - 3, 2)
            do(chain_r, GROUPS - 1, 1)
            do(chain_e, GROUPS - 1, 1)
            do(xn3_transposed, GROUPS - 2)
            do(chain_u, GROUPS - 1, 1)
            do(down, GROUPS - 3, 0)
            do(down, GROUPS - 3, 1)
            do(gate_up, GROUPS - 2, 0)
            do(gate_up, GROUPS - 2, 1)
            do(gate_up, GROUPS - 2, 2)
            do(xn3_transposed, GROUPS - 1, 0)
            do(xn3_transposed, GROUPS - 1, 1)
            do(gate_up, GROUPS - 1, 0, 0)
            do(gate_up, GROUPS - 1, 1, 0)
            do(gate_up, GROUPS - 1, 2, 0)
            do(down, GROUPS - 2, 0)
            do(down, GROUPS - 2, 1)
            do(gate_up, GROUPS - 1, 0, 1)
            do(gate_up, GROUPS - 1, 1, 1)
            do(gate_up, GROUPS - 1, 2, 1)
            do(down, GROUPS - 1, 0)
            do(down, GROUPS - 1, 1)
            keep_warm(3, ps_chain)


_NAMES = ["L0_attn_x", "L0_attn_W0", "L0_attn_Wkv", "L0_attn_bkv", "L0_attn_eta",
          "L0_ffn_w_gate", "L0_ffn_w_up", "L0_ffn_w_down"]


def kernel(**inputs):
    import numpy as np
    import concourse.bacc as bacc
    from concourse.bass_utils import run_bass_kernel_spmd

    nc = bacc.Bacc("TRN2", target_bir_lowering=False, num_devices=1)
    arrays, args = {}, []
    for name in _NAMES:
        a = np.ascontiguousarray(inputs[name])
        if a.ndim < 2:
            a = a.reshape(1, -1)
        arrays[name + "_dram"] = a
        args.append(nc.dram_tensor(name + "_dram", a.shape, mybir.dt.from_np(a.dtype), kind="ExternalInput").ap())
    shape = inputs["L0_attn_x"].shape
    out = nc.dram_tensor("out_dram", shape, F32, kind="ExternalOutput").ap()
    ttt_swiglu_kernel(nc, *args, out)
    result = run_bass_kernel_spmd(nc, [arrays], core_ids=[0])
    return result.results[0]["out_dram"]
```
